# Optimizing a Trainium2 kernel written in Bass

```python
import numpy as np
import jax
import jax.numpy as jnp

def _softmax(x, axis=-1):
    return jax.nn.softmax(x, axis=axis)

def _gelu(x):
    return jax.nn.gelu(x, approximate=True)

def _silu(x):
    return jax.nn.silu(x)

def _sigmoid(x):
    return jax.nn.sigmoid(x)

def _layernorm(x, axis=-1, eps=1e-05):
    m = jnp.mean(x, axis=axis, keepdims=True)
    v = jnp.var(x, axis=axis, keepdims=True)
    return (x - m) / jnp.sqrt(v + eps)

def _scatter_add(tgt, idx, src, axis=0):
    return tgt.at[idx].add(src)

def _segment_sum(src, seg, n):
    return jax.ops.segment_sum(src, seg, n)
kernel_name = 'mk_gnn_resnorm_d2_gnn_r8_e407fa'

def setup_inputs(seed: int=0):
    np.random.seed(seed)
    _w = jnp.asarray

    def _rec_inputs():
        import jax
        import jax.numpy as jnp
        _gk = jax.random.key(seed)
        x = -0.000929 + 1 * jax.random.normal(jax.random.fold_in(_gk, 1), (12500, 32), jnp.float32)
        src = jax.random.randint(jax.random.fold_in(_gk, 2), (400000,), 0, 12500, jnp.int32)
        dst = jax.random.randint(jax.random.fold_in(_gk, 3), (400000,), 0, 12500, jnp.int32)
        _o = jnp.argsort(dst, stable=True)
        src = src[_o]
        dst = dst[_o]
        edge_attr_4 = 0.00086875 + 0.999764 * jax.random.normal(jax.random.fold_in(_gk, 12), (400000, 4), jnp.float32)
        edge_attr_8 = jax.random.uniform(jax.random.fold_in(_gk, 13), (400000, 8), jnp.float32, 0.0, 1)
        return (x, src, dst, edge_attr_4, edge_attr_8)
    x, src, dst, edge_attr_4, edge_attr_8 = _rec_inputs()

    def _L0_gnn_setup():
        import jax, jax.numpy as jnp
        import numpy as np
        N = 4096
        E = 65536
        MUL = 8
        NB = 8
        HR = 64
        NTP = 4 * MUL * MUL
        AVG_NEI = 16.0
        INV_SQRT3 = 1.0 / np.sqrt(3.0)
        ALPHA = 1.0 / np.sqrt(2.0 * MUL)
        key = jax.random.key(seed)
        ks = jax.random.split(key, 12)
        h = jax.random.normal(ks[0], (N, 4 * MUL), jnp.float32)
        edge_index = jax.random.randint(ks[1], (2, E), 0, N)
        edge_sh = jax.random.normal(ks[2], (E, 4), jnp.float32)
        edge_radial = jax.random.uniform(ks[3], (E, NB), jnp.float32)

        def lin(k, fi, fo):
            return (jax.random.normal(k, (fi, fo), jnp.float32) / np.sqrt(fi)).astype(jnp.float32)
        W1 = lin(ks[4], NB, HR)
        b1 = jnp.zeros((HR,), jnp.float32)
        W2 = lin(ks[5], HR, HR)
        b2 = jnp.zeros((HR,), jnp.float32)
        W3 = lin(ks[6], HR, NTP)
        b3 = jnp.zeros((NTP,), jnp.float32)
        Ws = jax.random.normal(ks[7], (MUL, MUL), jnp.float32)
        Wv = jax.random.normal(ks[8], (MUL, MUL), jnp.float32)
        return dict(h=h, edge_index=edge_index, edge_sh=edge_sh, edge_radial=edge_radial, n_atoms=N, W1=W1, b1=b1, W2=W2, b2=b2, W3=W3, b3=b3, Ws=Ws, Wv=Wv)
    _L0_gnn_all = _L0_gnn_setup()
    _L0_gnn_in = {k: v for k, v in _L0_gnn_all.items() if k in ('W1', 'b1', 'W2', 'b2', 'W3', 'b3', 'Ws', 'Wv')}
    del _L0_gnn_all

    def _L1_gnn_setup():
        import jax, jax.numpy as jnp
        import numpy as np
        N_NODES = 12500
        N_EDGES = 200000
        DIM1 = 32
        LEAKY_SLOPE = 0.01
        key = jax.random.key(seed)
        k1, k2, k3, k4 = jax.random.split(key, 4)
        h = jax.random.normal(k1, (N_NODES, DIM1), dtype=jnp.float32)
        attn_w = jax.random.normal(k2, (2 * DIM1,), dtype=jnp.float32) * (1.0 / np.sqrt(2 * DIM1))
        src = jax.random.randint(k3, (N_EDGES,), 0, N_NODES, dtype=jnp.int32)
        dst = jax.random.randint(k4, (N_EDGES,), 0, N_NODES, dtype=jnp.int32)
        return {'h': h, 'attn_w': attn_w, 'src': src, 'dst': dst}
    _L1_gnn_all = _L1_gnn_setup()
    _L1_gnn_in = {k: v for k, v in _L1_gnn_all.items() if k in ('attn_w',)}
    del _L1_gnn_all
    return {'x': x, 'src': src, 'dst': dst, 'edge_attr_4': edge_attr_4, 'edge_attr_8': edge_attr_8, 'L0_gnn_W1': _L0_gnn_in['W1'], 'L0_gnn_b1': _L0_gnn_in['b1'], 'L0_gnn_W2': _L0_gnn_in['W2'], 'L0_gnn_b2': _L0_gnn_in['b2'], 'L0_gnn_W3': _L0_gnn_in['W3'], 'L0_gnn_b3': _L0_gnn_in['b3'], 'L0_gnn_Ws': _L0_gnn_in['Ws'], 'L0_gnn_Wv': _L0_gnn_in['Wv'], 'L1_gnn_attn_w': _L1_gnn_in['attn_w']}

def reference(x, src, dst, edge_attr_4, edge_attr_8, L0_gnn_W1, L0_gnn_b1, L0_gnn_W2, L0_gnn_b2, L0_gnn_W3, L0_gnn_b3, L0_gnn_Ws, L0_gnn_Wv, L1_gnn_attn_w):
    import jax
    import jax.numpy as jnp

    def _L0_gnn_ref(h, edge_index, edge_sh, edge_radial, n_atoms, W1, b1, W2, b2, W3, b3, Ws, Wv):
        import jax, jax.numpy as jnp
        import numpy as np
        N = 4096
        E = 65536
        MUL = 8
        NB = 8
        HR = 64
        NTP = 4 * MUL * MUL
        AVG_NEI = 16.0
        INV_SQRT3 = 1.0 / np.sqrt(3.0)
        ALPHA = 1.0 / np.sqrt(2.0 * MUL)
        src, dst = (edge_index[0], edge_index[1])
        x = jax.nn.silu(edge_radial @ W1 + b1)
        x = jax.nn.silu(x @ W2 + b2)
        tpw = x @ W3 + b3
        P = MUL * MUL
        W00 = tpw[:, 0 * P:1 * P].reshape(-1, MUL, MUL)
        W110 = tpw[:, 1 * P:2 * P].reshape(-1, MUL, MUL)
        W01 = tpw[:, 2 * P:3 * P].reshape(-1, MUL, MUL)
        W10 = tpw[:, 3 * P:4 * P].reshape(-1, MUL, MUL)
        hs = h[:, :MUL]
        hv = h[:, MUL:].reshape(-1, MUL, 3)
        hs_e = hs[src]
        hv_e = hv[src]
        sh0 = edge_sh[:, 0]
        sh1 = edge_sh[:, 1:4]
        m0 = ALPHA * (jnp.einsum('eu,euw->ew', hs_e * sh0[:, None], W00) + INV_SQRT3 * jnp.einsum('eui,ei,euw->ew', hv_e, sh1, W110))
        m1 = ALPHA * (jnp.einsum('eu,ei,euw->ewi', hs_e, sh1, W01) + jnp.einsum('eui,euw->ewi', hv_e * sh0[:, None, None], W10))
        messages = jnp.concatenate([m0, m1.reshape(-1, 3 * MUL)], axis=-1)
        agg = jax.ops.segment_sum(messages, dst, num_segments=n_atoms) / np.sqrt(AVG_NEI)
        self0 = hs @ Ws / np.sqrt(MUL)
        self1 = jnp.einsum('nui,uw->nwi', hv, Wv) / np.sqrt(MUL)
        h_self = jnp.concatenate([self0, self1.reshape(-1, 3 * MUL)], axis=-1)
        return h_self + agg

    def _L1_gnn_ref(h, attn_w, src, dst):
        import jax, jax.numpy as jnp
        import numpy as np
        N_NODES = 12500
        N_EDGES = 200000
        DIM1 = 32
        LEAKY_SLOPE = 0.01
        N, d = h.shape
        s_src = h @ attn_w[:d]
        s_dst = h @ attn_w[d:]
        e = s_src[src] + s_dst[dst]
        e = jnp.where(e >= 0, e, LEAKY_SLOPE * e)
        m = jax.ops.segment_max(e, dst, num_segments=N)
        ex = jnp.exp(e - m[dst])
        denom = jax.ops.segment_sum(ex, dst, num_segments=N)
        alpha = ex / denom[dst]
        out = jax.ops.segment_sum(h[src] * alpha[:, None], dst, num_segments=N)
        return out
    edge_index = jnp.stack([src, dst])
    x = _layernorm(x + _L0_gnn_ref(x, edge_index, edge_attr_4, edge_attr_8, 12500, L0_gnn_W1, L0_gnn_b1, L0_gnn_W2, L0_gnn_b2, L0_gnn_W3, L0_gnn_b3, L0_gnn_Ws, L0_gnn_Wv), axis=-1)
    x = _layernorm(x + _L1_gnn_ref(x, L1_gnn_attn_w, src, dst), axis=-1)
    return x

_drawn_inputs = setup_inputs


def setup_inputs(seed=0):
    import zlib

    import numpy as np

    out = dict(_drawn_inputs(seed))
    spreads = {'L0_gnn_b1': (0.0, 0.268), 'L0_gnn_b2': (0.0, 0.1), 'L0_gnn_b3': (0.0, 0.1)}
    factors = {}
    for name, (base, spread) in spreads.items():
        noise = np.random.default_rng([zlib.crc32(name.encode()), seed]).standard_normal(out[name].shape)
        drawn = base * np.exp(spread * noise) if base else spread * noise
        out[name] = jnp.asarray(drawn.astype(out[name].dtype))
    for name, factor in factors.items():
        out[name] = (out[name] * factor).astype(out[name].dtype)
    return out
```

```python
from contextlib import ExitStack

import concourse.bass as bass
from concourse import mybir

ALU = mybir.AluOpType
ACT = mybir.ActivationFunctionType
AX = mybir.AxisListType.X
F32 = mybir.dt.float32
I32 = mybir.dt.int32

P = 128
N, D = 12500, 32
E = 400000
T = E // P
MUL, NB, HR = 8, 8, 64
NTP = 4 * MUL * MUL
GT = 5
GC = GT * P
HC = GC // 2
SLOTS = 6
HALF = SLOTS // 2
ITERS = T // (GT * SLOTS)
QUARTERS = 4
CHUNKS = ITERS // QUARTERS
CT = QUARTERS * SLOTS * GT
LAST = ITERS * SLOTS
LAST_T = ITERS * SLOTS * GT
assert LAST_T + GT == T and CHUNKS * QUARTERS == ITERS and SLOTS % 2 == 0
NP_, NJ = 125, 100
FIRSTS = 800
ROW = E // FIRSTS
assert NP_ * NJ == N and ITERS >= NJ + 1
TW = D + 1
SW = D + 2
BT = 25
BLOCKS = T // BT
PAIRS = BLOCKS // 2
assert BLOCKS == 2 * PAIRS + 1
NBATCH = 4
BJ = NJ // NBATCH
SJ = 512 // D
TPAD = (ITERS + 1) * SLOTS * GT
assert (BLOCKS + 1) * BT <= TPAD
ABSENT = 1 << 20
BLOCK_STEPS = 6
BIG = 1.0e30
EPS = 1e-5


def build(nc, x, x_t, src, dst, dst_firsts, dst_edges, sh, radial_t, w1, b1, w2, b2, w3, b3, w_self,
          attn, base, out):
    dst_v = dst.rearrange("(p t) -> p t", p=P)
    dst_rows = dst.rearrange("(r c) -> r c", c=ROW)
    scan0 = nc.dram_tensor("scan0", (E, D), F32, kind="Internal").ap()
    scan1 = nc.dram_tensor("scan1", (E, SW), F32, kind="Internal").ap()
    table = nc.dram_tensor("table", (N, TW), F32, kind="Internal").ap()
    starts = nc.dram_tensor("starts", (E, 1), F32, kind="Internal").ap()
    scan0_v = scan0.rearrange("(p t) d -> p t d", p=P)
    scan1_v = scan1.rearrange("(p t) d -> p t d", p=P)
    starts_v = starts.rearrange("(p t) o -> p (t o)", p=P)
    table_v = table.rearrange("(p j) w -> p j w", p=NP_)
    out_v = out.rearrange("(p j) d -> p j d", p=NP_)

    with ExitStack() as ctx:
        def sb(name, shape, dt=F32):
            return ctx.enter_context(nc.sbuf_tensor(name, shape, dt))

        def pb(name, shape):
            return ctx.enter_context(nc.psum_tensor(name, shape, F32))

        def sem(name):
            return ctx.enter_context(nc.semaphore(name))

        w1s = sb("w1s", [NB, HR])
        b1s = sb("b1s", [P, 1])
        w2s = sb("w2s", [P, HR])
        b2s = sb("b2s", [HR, 1])
        w3s = sb("w3s", [P, NTP])
        wselfs = sb("wselfs", [D, D])
        attns = sb("attns", [P, 2 * D])
        bases = sb("bases", [P, 2])
        ident = sb("ident", [P, P])
        big = sb("big", [P, TPAD * 4])
        sh_v = big[:, :].rearrange("p (t k) -> p t k", k=4)
        xts = big[0:D, 0:N].rearrange("d (j p) -> d j p", j=NJ)
        pen = big[:, 0:T]
        fill = big[:, T:2 * T]
        filled = big[:, 2 * T:3 * T]
        spare = big[:, 3 * T:4 * T]
        dstf = sb("dstf", [P, T])
        keep = sb("keep", [P, T])
        xs = sb("xs", [P, NJ, D])
        idx = sb("idx", [P, SLOTS, GT], I32)
        rad = sb("rad", [NB, SLOTS, GC])
        sh0 = sb("sh0", [P, SLOTS * GT])
        rows = sb("rows", [P, SLOTS, GT, D])
        hid1 = sb("hid1", [P, GC])
        hid2 = sb("hid2", [P, 2, GC])
        amp = sb("amp", [P, 2, GT, MUL + D])
        bprod = sb("bprod", [P, GT, MUL, 3])
        prod_a = sb("prod_a", [P, GT, MUL, 2 * MUL])
        prod_b = sb("prod_b", [P, GT, 4, MUL, MUL])
        red = sb("red", [P, HALF * GT, 4, MUL])
        tmp = sb("tmp", [P, HALF * GT, MUL, 3])
        msgs = sb("msgs", [P, CT, D])
        sums = sb("sums", [P, CT, D])
        state = sb("state", [P, D])
        msgs_f = msgs[:, :, :].rearrange("p t d -> p (t d)")
        sums_f = sums[:, :, :].rearrange("p t d -> p (t d)")
        firsts = sb("firsts", [P, FIRSTS], I32)
        junk = sb("junk", [P, FIRSTS])
        node_a = sb("node_a", [P, 1])
        node_b = sb("node_b", [P, 1])
        acc_a = sb("acc_a", [P, 1])
        acc_b = sb("acc_b", [P, 1])
        row_i = sb("row_i", [P, 1], I32)
        dst_row = sb("dst_row", [P, ROW], I32)
        rows_all = sb("rows_all", [P, ITERS])
        cnt_all = sb("cnt_all", [P, ITERS])
        upto = [sb(f"upto{i}", [P, NJ + 1]) for i in range(2)]
        end_f = sb("end_f", [P, NJ])
        end_i = sb("end_i", [P, NJ], I32)
        start_i = sb("start_i", [P, NJ], I32)
        deg = sb("deg", [P, NJ])
        has = sb("has", [P, NJ])
        has_w = sb("has_w", [P, NJ])
        firsts_r = sb("firsts_r", [TW, P], I32)
        lasts_r = sb("lasts_r", [TW, P], I32)
        cont_r = sb("cont_r", [TW, P])
        chain_r = sb("chain_r", [TW, P])
        contpen_r = sb("contpen_r", [TW, P])
        chainpen_r = sb("chainpen_r", [TW, P])
        fcount = sb("fcount", [P, 1])
        first_i = sb("first_i", [P, 1], I32)
        cr = [sb(f"cr{i}", [TW, P]) for i in range(6)]
        carry = sb("carry", [P, 2, TW])
        ends = sb("ends", [P, 2, TW])
        edge_row = sb("edge_row", [P, SW])
        edge_new = sb("edge_new", [P, SW])
        pm = sb("pm", [P, 4])
        agg0 = msgs_f[:, 0:NJ * D].rearrange("p (j w) -> p j w", j=NJ)
        agg1 = msgs_f[:, 0:NJ * SW].rearrange("p (j w) -> p j w", j=NJ)
        h1 = sums_f[:, 0:NJ * TW].rearrange("p (j w) -> p j w", j=NJ)
        tval = sb("tval", [P, NJ])
        v = [sb(f"v{i}", [P, BJ, D]) for i in range(3)]
        q = [sb(f"q{i}", [P, BJ]) for i in range(6)]
        idx1 = sb("idx1", [P, 2, BT], I32)
        ring = sb("ring", [P, 2, BT, TW])
        score = sb("score", [P, 2, BT])
        diff = sb("diff", [P, 2, BT])
        expd = sb("expd", [P, 2, BT])
        wsum = sb("wsum", [P, BT, D])
        run = sb("run", [P, 2, BT + 1, SW])

        hid = pb("hid", [P, 2, 512])
        tpw = [pb(f"tpw{i}", [P, 3 * 512]) for i in range(2)]

        def tpw_v(b):
            return tpw[b][:, 0:GT * NTP].rearrange("p (t c) -> p t c", t=GT)

        weights_in, w3_in, edges_in, x_in = sem("weights_in"), sem("w3_in"), sem("edges_in"), sem("x_in")
        cleared, w3_scaled, starts_zeroed = sem("cleared"), sem("w3_scaled"), sem("starts_zeroed")
        row_cleared = sem("row_cleared")
        ident_base, ident_ready = sem("ident_base"), sem("ident_ready")
        idx_in = [sem(f"idx_in{i}") for i in range(2)]
        rad_in = [sem(f"rad_in{i}") for i in range(2)]
        rows_in = [sem(f"rows_in{i}") for i in range(SLOTS)]
        hid1_psum, hid1_ready = sem("hid1_psum"), sem("hid1_ready")
        hid2_psum, hid2_ready = sem("hid2_psum"), sem("hid2_ready")
        tpw_ready, tpw_used, rows_used = sem("tpw_ready"), sem("tpw_used"), sem("rows_used")
        sh0_ready, amp_ready = sem("sh0_ready"), sem("amp_ready")
        prod_a_ready, prod_b_ready = sem("prod_a_ready"), sem("prod_b_ready")
        bprod_ready, b_ready = sem("bprod_ready"), sem("b_ready")
        red_ready, m0_ready, tmp_ready = sem("red_ready"), sem("m0_ready"), sem("tmp_ready")
        m1_ready, sums_ready, sums_stored = sem("m1_ready"), sem("sums_ready"), sem("sums_stored")
        state_ready = sem("state_ready")
        search_step, row_ready, dst_row_in = sem("search_step"), sem("row_ready"), sem("dst_row_in")
        vec_step, masks_ready, nodes_ready = sem("vec_step"), sem("masks_ready"), sem("nodes_ready")
        to_pe, from_pe, to_act, from_act = sem("to_pe"), sem("from_pe"), sem("to_act"), sem("from_act")
        x_t_in, self_ready = sem("x_t_in"), sem("self_ready")
        edge_row_in, edge_row_out = sem("edge_row_in"), sem("edge_row_out")
        edge_new_ready = sem("edge_new_ready")
        batch_in = [[sem(f"batch{l}_in{i}") for i in range(NBATCH)] for l in range(2)]
        h1_ready, table_out, starts_out = sem("h1_ready"), sem("table_out"), sem("starts_out")
        fill_in, out_ready, out_stored = sem("fill_in"), sem("out_ready"), sem("out_stored")
        idx1_in = [sem(f"idx1_in{i}") for i in range(2)]
        ring_in = [sem(f"ring_in{i}") for i in range(2)]
        ring_used, block_step, exp_ready, row0_ready = sem("ring_used"), sem("block_step"), sem("exp_ready"), sem("row0_ready")
        run_ready, run_stored = sem("run_ready"), [sem(f"run_stored{i}") for i in range(2)]

        block = ctx.enter_context(nc.Block())

        @block.sync
        def _(sp):
            for h in range(2):
                sp.dma_start(idx[:, h * HALF:(h + 1) * HALF, :],
                             src[:, h * HALF * GT:(h + 1) * HALF * GT]).then_inc(idx_in[h], 16)
            for k in range(2):
                sp.dma_start(idx1[:, k, :], src[:, k * BT:(k + 1) * BT]).then_inc(idx1_in[k], 16)
            sp.dma_start(rad[:, 0:HALF, :], radial_t[:, 0:HALF * GC]).then_inc(rad_in[0], 16)
            sp.dma_start(w1s[:, :], w1).then_inc(weights_in, 16)
            sp.dma_start(b1s[HR:P, :], b1).then_inc(weights_in, 16)
            sp.dma_start(w2s[HR:P, :], w2).then_inc(weights_in, 16)
            sp.dma_start(b2s[:, :], b2).then_inc(weights_in, 16)
            sp.dma_start(bases[:, :], base).then_inc(weights_in, 16)
            sp.dma_start(firsts[:, :], dst_firsts.to_broadcast([P, FIRSTS])).then_inc(weights_in, 16)
            sp.wait_ge(cleared, 1)
            sp.dma_start(w3s[0:HR, :], w3).then_inc(w3_in, 16)
            sp.dma_start(w3s[HR:HR + 1, :], b3).then_inc(w3_in, 16)
            sp.wait_ge(cleared, 3)
            sp.dma_start(big[:, 0:4 * T], sh).then_inc(edges_in, 16)
            sp.dma_start(sums_f[:, 0:T].bitcast(I32), dst_v).then_inc(edges_in, 16)
            sp.dma_start(rad[:, HALF:SLOTS, :], radial_t[:, HALF * GC:SLOTS * GC]).then_inc(rad_in[1], 16)
            sp.dma_start(starts_v, msgs_f[:, 0:T]).then_inc(starts_zeroed, 16)
            sp.dma_start(firsts_r[:, :], dst_edges[0:1, :].to_broadcast([TW, P])).then_inc(edges_in, 16)
            sp.dma_start(lasts_r[:, :], dst_edges[1:2, :].to_broadcast([TW, P])).then_inc(edges_in, 16)
            sp.dma_start(wselfs[:, :], w_self).then_inc(x_in, 16)
            sp.dma_start(attns[:, :], attn.to_broadcast([P, 2 * D])).then_inc(x_in, 16)
            sp.dma_start(xs[0:NP_, :, :], x.rearrange("(p j) d -> p j d", p=NP_)).then_inc(x_in, 16)
            with sp.Fori(0, CHUNKS) as c:
                with sp.Fori(0, QUARTERS) as r:
                    it = c * QUARTERS + r
                    for h in range(2):
                        nxt = it * (SLOTS * GT) + (SLOTS + h * HALF) * GT
                        for k in range(h * HALF, (h + 1) * HALF):
                            sp.wait_ge(rows_in[k], it * (16 * GT) + 16 * GT)
                        sp.dma_start(idx[:, h * HALF:(h + 1) * HALF, :],
                                     src[:, bass.ds(nxt, HALF * GT)]).then_inc(idx_in[h], 16)
                        sp.wait_ge(hid1_psum, it * SLOTS + (h + 1) * HALF)
                        sp.dma_start(rad[:, h * HALF:(h + 1) * HALF, :],
                                     radial_t[:, bass.ds(nxt * P, HALF * GC)]).then_inc(rad_in[h], 16)
                sp.wait_ge(sums_ready, c + 1)
                sp.dma_start(scan0_v[:, bass.ds(c * CT, CT), :], sums[:, :, :]).then_inc(sums_stored, 16)
            sp.wait_ge(m1_ready, 2 * ITERS + 1)
            sp.wait_ge(amp_ready, LAST + 1)
            sp.dma_start(xts, x_t).then_inc(x_t_in, 16)
            sp.wait_ge(sums_ready, CHUNKS + 1)
            sp.dma_start(scan0_v[:, LAST_T:T, :], sums[:, 0:GT, :]).then_inc(sums_stored, 16)
            for b in range(NBATCH):
                sp.wait_ge(h1_ready, b + 1)
                sp.dma_start(table_v[:, b * BJ:(b + 1) * BJ, :],
                             h1[0:NP_, b * BJ:(b + 1) * BJ, :]).then_inc(table_out, 16)
            sp.wait_ge(starts_out, 16 * NJ)
            sp.wait_ge(self_ready, -(-NJ // SJ))
            sp.dma_start(fill, starts_v).then_inc(fill_in, 16)

            def next_block(b, pair, k):
                sp.wait_ge(ring_in[k], pair * (16 * BT) + 16 * BT)
                sp.dma_start(idx1[:, k, :], src[:, bass.ds(b * BT + 2 * BT, BT)]).then_inc(idx1_in[k], 16)

            def store_block(b, k):
                sp.wait_ge(run_ready, b + 1)
                sp.dma_start(scan1_v[:, bass.ds(b * BT, BT), :], run[:, k, 1:BT + 1, :])\
                  .then_inc(run_stored[k], 16)

            with sp.Fori(0, PAIRS) as pair:
                for k in range(2):
                    next_block(pair * 2 + k, pair, k)
                    store_block(pair * 2 + k, k)
            store_block(BLOCKS - 1, 0)
            for b in range(NBATCH):
                sp.wait_ge(out_ready, b + 1)
                sp.dma_start(out_v[:, b * BJ:(b + 1) * BJ, :],
                             xs[0:NP_, b * BJ:(b + 1) * BJ, :]).then_inc(out_stored, 16)
            sp.wait_ge(out_stored, 16 * NBATCH)
            sp.wait_ge(idx_in[1], 16 * (ITERS + 1))
            sp.wait_ge(rad_in[1], 16 * (ITERS + 1))
            sp.wait_ge(idx1_in[1], 16 * (PAIRS + 1))

        @block.gpsimd
        def _(pool):
            def gather(dest, source, index):
                return pool.indirect_dma_start(out=dest, out_offset=None, in_=source,
                                               in_offset=bass.IndirectOffsetOnAxis(ap=index, axis=0))

            def scatter(dest, source, index):
                return pool.indirect_dma_start(out=dest, in_=source, in_offset=None,
                                               out_offset=bass.IndirectOffsetOnAxis(ap=index, axis=0),
                                               bounds_check=E - 1, oob_is_err=False)

            def gather_group(it, k):
                pool.wait_ge(rows_used, it * SLOTS + k + 1)
                pool.wait_ge(idx_in[k // HALF], it * 16 + 16)
                pool.nop(nofuse=True)
                for t in range(GT):
                    gather(rows[:, k, t, :], x[:, :], idx[:, k, t:t + 1]).then_inc(rows_in[k], 16)

            def gather_block(b, pair, k):
                pool.wait_ge(ring_used, b + 1)
                pool.wait_ge(idx1_in[k], pair * 16 + 16)
                pool.nop(nofuse=True)
                for t in range(BT):
                    gather(ring[:, k, t, :], table[:, :], idx1[:, k, t:t + 1]).then_inc(ring_in[k], 16)

            def patch(scan, width, layer):
                gather(edge_row[:, 0:width], scan[:, :], first_i[:, :]).then_inc(edge_row_in, 16)
                pool.wait_ge(edge_new_ready, layer + 1)
                scatter(scan[:, :], edge_new[:, 0:width], first_i[:, :]).then_inc(edge_row_out, 16)
                pool.wait_ge(edge_row_out, 16 * (layer + 1))

            def gather_nodes(agg, scan, layer):
                for j in range(NJ):
                    gather(agg[:, j, :], scan[:, :], end_i[:, j:j + 1])\
                        .then_inc(batch_in[layer][j // BJ], 16)

            pool.memset(row_i[:, :], 0).then_inc(row_cleared, 1)
            pool.wait_ge(row_cleared, 1)
            gather(dst_row[:, :], dst_rows[:, :], row_i[:, :]).then_inc(dst_row_in, 16)
            with pool.Fori(0, ITERS) as it:
                for k in range(SLOTS):
                    gather_group(it, k)
                pool.wait_ge(row_ready, it + 1)
                pool.nop(nofuse=True)
                gather(dst_row[:, :], dst_rows[:, :], row_i[:, :]).then_inc(dst_row_in, 16)
            gather_group(ITERS, 0)
            pool.memset(ident[:, :], 0.0).then_inc(ident_base, 1)
            pool.wait_ge(ident_base, 1)
            pool.affine_select(out=ident[:, :], in_=ident[:, :], compare_op=ALU.not_equal, fill=1.0,
                               base=0, pattern=[[-1, P]], channel_multiplier=1).then_inc(ident_ready, 1)
            pool.wait_ge(masks_ready, 1)
            pool.wait_ge(sums_stored, 16 * (CHUNKS + 2))
            patch(scan0, D, 0)
            pool.wait_ge(nodes_ready, 1)
            gather_nodes(agg0, scan0, 0)
            pool.wait_ge(starts_zeroed, 16)
            for j in range(NJ):
                if j % BJ == 0:
                    pool.wait_ge(h1_ready, j // BJ + 1)
                scatter(starts[:, :], tval[:, j:j + 1], start_i[:, j:j + 1]).then_inc(starts_out, 16)
            pool.wait_ge(table_out, 16 * NBATCH)
            with pool.Fori(0, PAIRS) as pair:
                for k in range(2):
                    gather_block(pair * 2 + k, pair, k)
            gather_block(BLOCKS - 1, PAIRS, 0)
            pool.wait_ge(run_stored[0], 16 * (PAIRS + 2))
            pool.wait_ge(run_stored[1], 16 * (PAIRS + 1))
            patch(scan1, SW, 1)
            gather_nodes(agg1, scan1, 1)

        @block.tensor
        def _(pe):
            def layer1(g, it, k):
                pe.wait_ge(rad_in[k // HALF], it * 16 + 16)
                pe.wait_ge(hid1_ready, g + 1)
                for h in range(2):
                    mm = pe.matmul(hid[HR:P, h, 0:HC], w1s[:, :], rad[:, k, h * HC:(h + 1) * HC],
                                   start=True, stop=True)
                mm.then_inc(hid1_psum, 1)

            def layer2(g):
                pe.wait_ge(hid1_ready, g + 2)
                pe.wait_ge(hid2_ready, g + 1)
                pe.nop(nofuse=True)
                for h in range(2):
                    mm = pe.matmul(hid[0:HR, h, 0:HC], w2s[HR:P, :], hid1[HR:P, h * HC:(h + 1) * HC],
                                   start=True, stop=True)
                mm.then_inc(hid2_psum, 1)

            def layer3(g, b, tiles):
                if tiles[0] == 0:
                    pe.wait_ge(hid2_ready, g + 2)
                    pe.wait_ge(tpw_used, g + 1)
                for t in tiles:
                    mm = pe.matmul(tpw_v(b)[:, t, :], hid2[:, b, t * P:(t + 1) * P], w3s[:, :],
                                   start=True, stop=True)
                if tiles[-1] == GT - 1:
                    mm.then_inc(tpw_ready, 1)

            pe.wait_ge(weights_in, 16 * 6)
            pe.wait_ge(w3_scaled, 1)
            layer1(0, 0, 0)
            layer2(0)
            with pe.Fori(0, ITERS) as it:
                for k in range(SLOTS):
                    g = it * SLOTS + k
                    nxt = (it + 1) if k == SLOTS - 1 else it
                    layer1(g + 1, nxt, (k + 1) % SLOTS)
                    layer3(g, k % 2, range(0, 3))
                    layer2(g + 1)
                    layer3(g, k % 2, range(3, GT))
            layer3(LAST, 0, range(0, 3))
            layer3(LAST, 0, range(3, GT))

            turns = [0]

            def turn(out_ap, in_ap, size):
                turns[0] += 1
                pe.wait_ge(to_pe, turns[0])
                pe.transpose(out_ap, in_ap, ident[0:size, 0:size]).then_inc(from_pe, 1)

            pe.wait_ge(ident_ready, 1)
            turn(hid[0:D, 1, 0:P], state[:, :], P)
            turn(hid[:, 1, 0:D], cr[2][0:D, :], D)
            pe.wait_ge(x_t_in, 16)
            pe.wait_ge(x_in, 16 * 3)
            pe.wait_ge(tpw_used, LAST + 3)
            for j in range(NJ):
                bank, at = j // SJ, j % SJ
                bank_ap = hid[:, 0, :] if bank == 6 else tpw[bank // 3][:, (bank % 3) * 512:(bank % 3 + 1) * 512]
                mm = pe.matmul(bank_ap[0:NP_, at * D:(at + 1) * D], xts[:, j, :], wselfs[:, :],
                               start=True, stop=True)
                if at == SJ - 1 or j == NJ - 1:
                    mm.then_inc(self_ready, 1)
            turn(hid[0:1, 1, 0:P], filled[:, T - 1:T], P)
            turn(hid[:, 1, 0:1], cr[2][0:1, :], 1)
            turn(hid[0:TW, 1, 0:P], ends[:, 0, :], P)
            turn(hid[0:TW, 1, P:2 * P], ends[:, 1, :], P)
            turn(hid[:, 1, 0:TW], cr[5][:, :], TW)
            turn(hid[:, 1, P:P + TW], cr[4][:, :], TW)

        @block.scalar
        def _(act):
            steps = 6

            def silu(dest, part, bias, done):
                act.activation(dest.rearrange("p (h c) -> p h c", h=2), part[:, :, 0:HC], ACT.Silu,
                               bias=bias).then_inc(done, 1)

            def hidden(g, b, after=()):
                act.wait_ge(hid1_psum, g + 1)
                act.wait_ge(hid2_psum, g + 1)
                silu(hid1[HR:P, :], hid[HR:P, :, :], b1s[HR:P, :], hid1_ready)
                for part in after:
                    part()
                act.wait_ge(hid2_psum, g + 2)
                silu(hid2[0:HR, b, :], hid[0:HR, :, :], b2s[:, :], hid2_ready)

            def spread_sh0(tile, h):
                act.activation(sh0[:, h * HALF * GT:(h + 1) * HALF * GT],
                               sh_v[:, bass.ds(tile, HALF * GT), 0], ACT.Copy).then_inc(sh0_ready, 1)

            def amplitudes(g, it, k, b, spread):
                act.wait_ge(rows_in[k], it * (16 * GT) + 16 * GT)
                act.wait_ge(tpw_used, g + 1)
                act.wait_ge(sh0_ready, spread)
                for t in range(GT):
                    a = act.activation(amp[:, b, t, MUL:], rows[:, k, t, :], ACT.Copy,
                                       scale=sh0[:, k * GT + t:k * GT + t + 1])
                a.then_inc(amp_ready, 1)

            def search(it):
                n = it * steps
                act.wait_ge(search_step, n + 2)
                act.wait_ge(dst_row_in, it * 16 + 16)
                act.activation(junk[:, 0:ROW], dst_row[:, :], ACT.Sign, bias=node_b[:, :], scale=-1.0,
                               accum_out=acc_b[:, :]).then_inc(search_step, 1)
                act.wait_ge(search_step, n + 3)
                act.activation(junk[:, :], firsts[:, :], ACT.Sign, bias=node_a[:, :], scale=-1.0,
                               accum_out=acc_a[:, :]).then_inc(search_step, 1)
                act.activation(cnt_all[:, bass.ds(it, 1)], acc_b[:, :], ACT.Copy).then_inc(search_step, 1)
                act.wait_ge(search_step, n + 5)
                act.activation(acc_b[:, :], acc_a[:, :], ACT.Copy, scale=0.5, bias=FIRSTS / 2 - 1.0)\
                   .then_inc(search_step, 1)
                act.wait_ge(search_step, n + 6)
                act.activation(rows_all[:, bass.ds(it, 1)], acc_b[:, :], ACT.Relu)
                act.activation(row_i[:, :], acc_b[:, :], ACT.Relu).then_inc(row_ready, 1)
                act.activation(node_b[:, :], node_a[:, :], ACT.Copy).then_inc(search_step, 1)
                act.wait_ge(search_step, n + 7)
                act.activation(node_a[:, :], node_a[:, :], ACT.Copy, bias=1.0).then_inc(search_step, 1)

            act.wait_ge(weights_in, 16 * 6)
            act.activation(node_a[:, :], bases[:, 1:2], ACT.Copy).then_inc(search_step, 1)
            act.activation(node_b[:, :], bases[:, 1:2], ACT.Copy).then_inc(search_step, 1)
            act.wait_ge(edges_in, 16 * 4)
            spread_sh0(0, 0)
            act.wait_ge(cleared, 4)
            hidden(0, 0, [lambda: amplitudes(0, 0, 0, 0, 1)])
            with act.Fori(0, ITERS) as it:
                for k in range(SLOTS):
                    g = it * SLOTS + k
                    nxt, kn = ((it + 1) if k == SLOTS - 1 else it), (k + 1) % SLOTS
                    parts = [lambda: amplitudes(g + 1, nxt, kn, kn % 2, nxt * 2 + 1 + kn // HALF)]
                    if k == 1:
                        parts.insert(0, lambda: spread_sh0(it * (SLOTS * GT) + HALF * GT, 1))
                    if k == SLOTS - 2:
                        parts.insert(0, lambda: spread_sh0(it * (SLOTS * GT) + SLOTS * GT, 0))
                    if k == HALF:
                        parts.append(lambda: search(it))
                    hidden(g + 1, kn % 2, parts)

            turns = [0]

            def apply(out_ap, in_ap, function):
                turns[0] += 1
                act.wait_ge(to_act, turns[0])
                act.activation(out_ap, in_ap, function).then_inc(from_act, 1)

            for b in range(NBATCH):
                apply(q[3][0:NP_, :], q[2][0:NP_, :], ACT.Sqrt)

            def exponents(b):
                act.wait_ge(block_step, b * BLOCK_STEPS + 6)
                act.activation(expd[:, :, :], diff[:, :, :], ACT.Exp).then_inc(exp_ready, 1)

            with act.Fori(0, BLOCKS) as b:
                exponents(b)
            apply(cr[3][:, :], cr[3][:, :], ACT.Exp)
            apply(cr[4][:, :], cr[4][:, :], ACT.Exp)
            apply(pm[:, 1:3], pm[:, 1:3], ACT.Exp)
            for b in range(NBATCH):
                apply(q[3][0:NP_, :], q[2][0:NP_, :], ACT.Sqrt)

        @block.vector
        def _(dve):
            done = [0]

            def link(ins):
                done[0] += 1
                ins.then_inc(vec_step, 1)
                dve.wait_ge(vec_step, done[0])

            asked = {"pe": 0, "act": 0}

            def turned(n=1):
                asked["pe"] += n
                dve.wait_ge(from_pe, asked["pe"])

            def applied(n=1):
                asked["act"] += n
                dve.wait_ge(from_act, asked["act"])

            dve.memset(w3s[:, :], 0.0).then_inc(cleared, 1)
            dve.memset(msgs_f[:, :], 0.0).then_inc(cleared, 1)
            dve.memset(big[:, 4 * T:4 * TPAD], 0.0).then_inc(cleared, 1)
            link(dve.memset(hid2[:, :, :], 0.0))
            dve.memset(hid2[HR:HR + 1, :, :], 1.0).then_inc(cleared, 1)
            dve.sem_inc(rows_used, SLOTS)
            dve.sem_inc(tpw_used, 2)
            dve.sem_inc(hid1_ready, 1)
            dve.sem_inc(hid2_ready, 1)
            dve.sem_inc(hid2_psum, 1)
            dve.sem_inc(sums_stored, 16)
            dve.sem_inc(ring_used, 2)
            for k in range(2):
                dve.sem_inc(run_stored[k], 16)
            dve.wait_ge(w3_in, 32)
            w110 = w3s[:, 0:2 * MUL * MUL].rearrange("p (w u) -> p w u", w=MUL)[:, :, 0:MUL]
            dve.tensor_scalar(w110, w110, 1.0 / 3.0 ** 0.5, None, ALU.mult).then_inc(w3_scaled, 1)
            dve.wait_ge(edges_in, 16 * 4)
            link(dve.tensor_copy(dstf[:, :], sums_f[:, 0:T].bitcast(I32)))
            dve.memset(keep[:, 0:1], 0.0)
            link(dve.tensor_tensor(keep[:, 1:T], dstf[:, 1:T], dstf[:, 0:T - 1], ALU.is_equal))
            link(dve.memset(state[:, :], 0.0))
            dve.wait_ge(starts_zeroed, 16)

            def bsum(g, it, k, b):
                dve.wait_ge(rows_in[k], it * (16 * GT) + 16 * GT)
                dve.tensor_tensor(
                    bprod[:, :, :, :], rows[:, k, :, MUL:].rearrange("p t (u i) -> p t u i", i=3),
                    sh_v[:, bass.ds(g * GT, GT), 1:4].unsqueeze(2).to_broadcast([P, GT, MUL, 3]),
                    ALU.mult).then_inc(bprod_ready, 1)

            def bsum_end(g, b):
                dve.wait_ge(bprod_ready, g + 1)
                dve.tensor_reduce(amp[:, b, :, 0:MUL], bprod[:, :, :, :], AX, ALU.add).then_inc(b_ready, 1)

            def products(g, k, b):
                w = tpw_v(b)
                dve.wait_ge(tpw_ready, g + 1)
                dve.wait_ge(amp_ready, g + 1)
                dve.wait_ge(b_ready, g + 1)
                dve.tensor_tensor(
                    prod_a[:, :, :, :],
                    w[:, :, 0:2 * MUL * MUL].rearrange("p t (w u) -> p t w u", w=MUL),
                    amp[:, b, :, 0:2 * MUL].unsqueeze(2).to_broadcast([P, GT, MUL, 2 * MUL]),
                    ALU.mult).then_inc(prod_a_ready, 1)
                dve.tensor_tensor(
                    prod_b[:, :, 0, :, :],
                    w[:, :, 2 * MUL * MUL:3 * MUL * MUL].rearrange("p t (w u) -> p t w u", w=MUL),
                    rows[:, k, :, 0:MUL].unsqueeze(2).to_broadcast([P, GT, MUL, MUL]),
                    ALU.mult).then_inc(rows_used, 1)
                hv = amp[:, b, :, 2 * MUL:].rearrange("p t (u i) -> p t i u", i=3)
                for i in range(3):
                    last = dve.tensor_tensor(
                        prod_b[:, :, 1 + i, :, :],
                        w[:, :, 3 * MUL * MUL:].rearrange("p t (w u) -> p t w u", w=MUL),
                        hv[:, :, i, :].unsqueeze(2).to_broadcast([P, GT, MUL, MUL]), ALU.mult)
                last.then_inc(tpw_used, 1)

            def reduce_a(g, tile):
                dve.wait_ge(prod_a_ready, g + 1)
                dve.tensor_reduce(msgs[:, bass.ds(tile, GT), 0:MUL], prod_a[:, :, :, :], AX, ALU.add)\
                   .then_inc(m0_ready, 1)

            def reduce_b(g, at):
                dve.wait_ge(tpw_used, g + 3)
                dve.tensor_reduce(red[:, at:at + GT, :, :].rearrange("p t c w -> p (t c w)"),
                                  prod_b[:, :, :, :, :].rearrange("p t c w u -> p (t c w) u"),
                                  AX, ALU.add).then_inc(red_ready, 1)

            def vectors(g, n, tile, sh_tile, tiles):
                dve.wait_ge(red_ready, g + 1)
                dve.tensor_tensor(
                    tmp[:, 0:tiles, :, :],
                    red[:, 0:tiles, 0, :].unsqueeze(3).to_broadcast([P, tiles, MUL, 3]),
                    sh_v[:, bass.ds(sh_tile, tiles), 1:4].unsqueeze(2).to_broadcast([P, tiles, MUL, 3]),
                    ALU.mult).then_inc(tmp_ready, 1)
                dve.wait_ge(tmp_ready, n + 1)
                dve.tensor_tensor(
                    msgs[:, bass.ds(tile, tiles), MUL:].rearrange("p t (w i) -> p t w i", i=3),
                    tmp[:, 0:tiles, :, :], red[:, 0:tiles, 1:4, :].rearrange("p t i w -> p t w i"),
                    ALU.add).then_inc(m1_ready, 1)

            def scans(c, halves, groups, tiles):
                dve.wait_ge(m1_ready, halves)
                dve.wait_ge(m0_ready, groups)
                dve.wait_ge(state_ready, c + 1)
                dve.wait_ge(sums_stored, c * 16 + 16)
                for f in range(D):
                    last = dve.tensor_tensor_scan(
                        sums[:, 0:tiles, f], keep[:, bass.ds(c * CT, tiles)], msgs[:, 0:tiles, f],
                        state[:, f:f + 1], ALU.mult, ALU.add)
                last.then_inc(sums_ready, 1)
                dve.wait_ge(sums_ready, c + 1)
                dve.tensor_copy(state[:, :], sums[:, tiles - 1, :]).then_inc(state_ready, 1)

            dve.sem_inc(state_ready, 1)
            bsum(0, 0, 0, 0)
            bsum_end(0, 0)
            with dve.Fori(0, CHUNKS) as c:
                with dve.Fori(0, QUARTERS) as r:
                    it = c * QUARTERS + r
                    for k in range(SLOTS):
                        g = it * SLOTS + k
                        nxt, kn = ((it + 1) if k == SLOTS - 1 else it), (k + 1) % SLOTS
                        products(g, k, k % 2)
                        reduce_a(g, r * (SLOTS * GT) + k * GT)
                        bsum(g + 1, nxt, kn, kn % 2)
                        reduce_b(g, (k % HALF) * GT)
                        bsum_end(g + 1, kn % 2)
                        if k % HALF == HALF - 1:
                            h = k // HALF
                            vectors(g, it * 2 + h, r * (SLOTS * GT) + h * HALF * GT,
                                    it * (SLOTS * GT) + h * HALF * GT, HALF * GT)
                scans(c, c * (2 * QUARTERS) + 2 * QUARTERS, c * (QUARTERS * SLOTS) + QUARTERS * SLOTS, CT)
            products(LAST, 0, 0)
            reduce_a(LAST, 0)
            reduce_b(LAST, 0)
            vectors(LAST, 2 * ITERS, 0, LAST_T, GT)
            scans(CHUNKS, 2 * ITERS + 1, LAST + 1, GT)

            dve.wait_ge(state_ready, CHUNKS + 2)
            dve.sem_inc(to_pe, 1)
            link(dve.memset(cont_r[:, 0:1], 0.0))
            link(dve.tensor_tensor(cont_r[:, 1:P], firsts_r[:, 1:P], lasts_r[:, 0:P - 1], ALU.is_equal))
            link(dve.tensor_tensor(chain_r[:, :], firsts_r[:, :], lasts_r[:, :], ALU.is_equal))
            link(dve.tensor_tensor(chain_r[:, :], chain_r[:, :], cont_r[:, :], ALU.mult))
            dve.tensor_scalar(contpen_r[:, :], cont_r[:, :], BIG, -BIG, ALU.mult, ALU.add)
            link(dve.tensor_scalar(chainpen_r[:, :], chain_r[:, :], BIG, -BIG, ALU.mult, ALU.add))
            link(dve.tensor_scalar(msgs_f[:, 0:T], dstf[:, :], dstf[:, 0:1], 0.0, ALU.is_equal, ALU.add,
                                   accum_out=fcount[:, :]))
            dve.scalar_tensor_tensor(out=first_i[:, :], in0=fcount[:, :], scalar=-1.0, in1=bases[:, 0:1],
                                     op0=ALU.add, op1=ALU.add).then_inc(masks_ready, 1)

            def carry_sums(width):
                turned()
                link(dve.tensor_copy(cr[0][0:width, :], hid[0:width, 1, 0:P]))
                link(dve.tensor_tensor_scan(cr[1][0:width, :], chain_r[0:width, :], cr[0][0:width, :],
                                            0.0, ALU.mult, ALU.add))
                link(dve.memset(cr[2][0:width, 0:1], 0.0))
                link(dve.tensor_tensor(cr[2][0:width, 1:P], cr[1][0:width, 0:P - 1],
                                       cont_r[0:width, 1:P], ALU.mult))
                dve.sem_inc(to_pe, 1)
                turned()

            carry_sums(D)
            dve.wait_ge(edge_row_in, 16)
            dve.tensor_tensor(edge_new[:, 0:D], edge_row[:, 0:D], hid[:, 1, 0:D], ALU.add)\
               .then_inc(edge_new_ready, 1)

            dve.wait_ge(search_step, 2 + 6 * ITERS)
            link(dve.tensor_scalar(upto[0][:, :], cnt_all[:, 1:NJ + 2], 0.5, ROW / 2.0, ALU.mult, ALU.add))
            link(dve.scalar_tensor_tensor(out=upto[1][:, :], in0=rows_all[:, 0:NJ + 1], scalar=float(ROW),
                                          in1=upto[0][:, :], op0=ALU.mult, op1=ALU.add))
            link(dve.tensor_scalar(end_i[:, :], upto[1][:, 1:], -1.0, 0.0, ALU.add, ALU.max))
            dve.sem_inc(nodes_ready, 1)
            link(dve.tensor_tensor(deg[:, :], upto[1][:, 1:], upto[1][:, 0:NJ], ALU.subtract))
            link(dve.tensor_scalar(has[:, :], deg[:, :], 1.0, None, ALU.min))
            link(dve.tensor_scalar(has_w[:, :], has[:, :], 1.0 / 16.0, None, ALU.mult))
            link(dve.tensor_scalar(end_f[:, :], has[:, :], -float(ABSENT), float(ABSENT), ALU.mult, ALU.add))
            link(dve.tensor_tensor(start_i[:, :], upto[1][:, 0:NJ], end_f[:, :], ALU.add))
            link(dve.memset(tval[:, :], 0.0))

            dve.wait_ge(x_in, 16 * 3)
            for bank in range(-(-NJ // SJ)):
                dve.wait_ge(self_ready, bank + 1)
                cols = min(SJ, NJ - bank * SJ)
                bank_ap = hid[:, 0, :] if bank == 6 else tpw[bank // 3][:, (bank % 3) * 512:(bank % 3 + 1) * 512]
                part = xs[0:NP_, bank * SJ:bank * SJ + cols, :].rearrange("p j d -> p (j d)")
                last = dve.scalar_tensor_tensor(out=part, in0=bank_ap[0:NP_, 0:cols * D],
                                                scalar=1.0 / MUL ** 0.5, in1=part,
                                                op0=ALU.mult, op1=ALU.add)
            link(last)
            link(dve.tensor_scalar(pen, keep[:, :], BIG, -BIG, ALU.mult, ALU.add))

            def bc(a):
                return a.unsqueeze(2).to_broadcast([NP_, BJ, D])

            vv = [a[0:NP_, :, :] for a in v]
            qq = [a[0:NP_, :] for a in q]

            def layernorm(dest):
                link(dve.tensor_reduce(qq[0], vv[1], AX, ALU.add))
                link(dve.tensor_scalar(qq[1], qq[0], 1.0 / D, None, ALU.mult))
                link(dve.tensor_tensor(vv[0], vv[1], bc(qq[1]), ALU.subtract))
                link(dve.tensor_tensor(vv[2], vv[0], vv[0], ALU.mult))
                link(dve.tensor_reduce(qq[0], vv[2], AX, ALU.add))
                link(dve.tensor_scalar(qq[2], qq[0], 1.0 / D, EPS, ALU.mult, ALU.add))
                dve.sem_inc(to_act, 1)
                applied()
                link(dve.reciprocal(qq[4], qq[3]))
                return dve.tensor_tensor(dest, vv[0], bc(qq[4]), ALU.mult)

            for b in range(NBATCH):
                js = slice(b * BJ, (b + 1) * BJ)
                dve.wait_ge(batch_in[0][b], 16 * BJ)
                link(dve.tensor_tensor(vv[0], agg0[0:NP_, js, :], bc(has_w[0:NP_, js]), ALU.mult))
                link(dve.tensor_tensor(vv[1], vv[0], xs[0:NP_, js, :], ALU.add))
                link(layernorm(h1[0:NP_, js, 0:D]))
                for a, dest in ((0, h1[0:NP_, js, D:TW].rearrange("p j o -> p (j o)")), (1, tval[0:NP_, js])):
                    link(dve.tensor_tensor(
                        vv[2], h1[0:NP_, js, 0:D],
                        attns[0:NP_, a * D:(a + 1) * D].unsqueeze(1).to_broadcast([NP_, BJ, D]), ALU.mult))
                    link(dve.tensor_reduce(dest, vv[2], AX, ALU.add))
                dve.sem_inc(h1_ready, 1)

            dve.wait_ge(fill_in, 16)
            link(dve.tensor_tensor_scan(filled, keep[:, :], fill, 0.0, ALU.mult, ALU.add))
            dve.sem_inc(to_pe, 1)
            carry_sums(1)
            link(dve.tensor_copy(carry[:, 0, 0:1], hid[:, 1, 0:1]))
            link(dve.tensor_scalar(spare, dstf[:, :], dstf[:, 0:1], carry[:, 0, 0:1], ALU.is_equal, ALU.mult))
            link(dve.tensor_tensor(filled, filled, spare, ALU.add))

            link(dve.memset(run[:, 0, 0, :], 0.0))
            link(dve.memset(run[:, 0, 0, SW - 1:SW], -BIG))
            dve.sem_inc(row0_ready, 1)

            def softmax_block(b, pair, k):
                n = b * BLOCK_STEPS
                edges = bass.ds(b * BT, BT)
                top = run[:, k, :, SW - 1]
                dve.wait_ge(ring_in[k], pair * (16 * BT) + 16 * BT)
                dve.tensor_tensor(score[:, 0, :], ring[:, k, :, D], filled[:, edges], ALU.add)\
                   .then_inc(block_step, 1)
                dve.wait_ge(block_step, n + 1)
                dve.scalar_tensor_tensor(out=score[:, 1, :], in0=score[:, 0, :], scalar=0.01,
                                         in1=score[:, 0, :], op0=ALU.mult, op1=ALU.max)\
                   .then_inc(block_step, 1)
                dve.wait_ge(block_step, n + 2)
                dve.wait_ge(run_stored[k], pair * 16 + 16)
                dve.wait_ge(row0_ready, b + 1)
                dve.tensor_tensor_scan(top[:, 1:], pen[:, edges], score[:, 1, :], top[:, 0:1],
                                       ALU.add, ALU.max).then_inc(block_step, 1)
                dve.wait_ge(block_step, n + 3)
                dve.tensor_tensor(diff[:, 0, :], top[:, 0:BT], pen[:, edges], ALU.add)\
                   .then_inc(block_step, 1)
                dve.tensor_tensor(diff[:, 1, :], score[:, 1, :], top[:, 1:], ALU.subtract)\
                   .then_inc(block_step, 1)
                dve.wait_ge(block_step, n + 4)
                dve.tensor_tensor(diff[:, 0, :], diff[:, 0, :], top[:, 1:], ALU.subtract)\
                   .then_inc(block_step, 1)
                dve.wait_ge(exp_ready, b + 1)
                dve.tensor_tensor(wsum[:, :, :], ring[:, k, :, 0:D],
                                  expd[:, 1, :].unsqueeze(2).to_broadcast([P, BT, D]), ALU.mult)\
                   .then_inc(ring_used, 1)
                dve.wait_ge(ring_used, b + 3)
                for f in range(D + 1):
                    added = expd[:, 1, :] if f == D else wsum[:, :, f]
                    last = dve.tensor_tensor_scan(run[:, k, 1:, f], expd[:, 0, :], added,
                                                  run[:, k, 0, f:f + 1], ALU.mult, ALU.add)
                last.then_inc(run_ready, 1)
                dve.wait_ge(run_ready, b + 1)
                dve.tensor_copy(run[:, 1 - k, 0, :], run[:, k, BT, :]).then_inc(row0_ready, 1)

            with dve.Fori(0, PAIRS) as pair:
                for k in range(2):
                    softmax_block(pair * 2 + k, pair, k)
            softmax_block(BLOCKS - 1, PAIRS, 0)

            dve.wait_ge(row0_ready, BLOCKS + 1)
            end = run[:, 1, 0, :]
            dve.tensor_copy(ends[:, 0, :], end[:, 0:TW])
            link(dve.tensor_copy(ends[:, 1, :], end[:, SW - 1:SW].to_broadcast([P, TW])))
            dve.sem_inc(to_pe, 2)
            turned(2)
            val, mx, cum, old, new, tot = (a[:, :] for a in cr)
            link(dve.tensor_copy(mx, hid[0:TW, 1, P:2 * P]))
            link(dve.tensor_copy(val, hid[0:TW, 1, 0:P]))
            link(dve.tensor_tensor_scan(cum, chainpen_r[:, :], mx, -BIG, ALU.add, ALU.max))
            link(dve.memset(old[:, 0:1], -BIG))
            link(dve.tensor_tensor(old[:, 1:P], cum[:, 0:P - 1], chainpen_r[:, 1:P], ALU.add))
            link(dve.tensor_tensor(old, old, cum, ALU.subtract))
            link(dve.tensor_tensor(new, mx, cum, ALU.subtract))
            dve.sem_inc(to_act, 2)
            applied(2)
            link(dve.tensor_tensor(tot, new, val, ALU.mult))
            link(dve.tensor_tensor_scan(val, old, tot, 0.0, ALU.mult, ALU.add))
            link(dve.memset(tot[:, 0:1], 0.0))
            link(dve.memset(new[:, 0:1], -BIG))
            link(dve.tensor_tensor(tot[:, 1:P], val[:, 0:P - 1], cont_r[:, 1:P], ALU.mult))
            link(dve.tensor_tensor(new[:, 1:P], cum[:, 0:P - 1], contpen_r[:, 1:P], ALU.add))
            dve.sem_inc(to_pe, 2)
            turned(2)
            link(dve.tensor_copy(carry[:, 0, :], hid[:, 1, 0:TW]))
            link(dve.tensor_copy(carry[:, 1, :], hid[:, 1, P:P + TW]))
            dve.wait_ge(edge_row_in, 32)
            dve.wait_ge(edge_row_out, 16)
            link(dve.tensor_tensor(pm[:, 0:1], edge_row[:, SW - 1:SW], carry[:, 1, 0:1], ALU.max))
            link(dve.tensor_tensor(pm[:, 1:2], edge_row[:, SW - 1:SW], pm[:, 0:1], ALU.subtract))
            link(dve.tensor_tensor(pm[:, 2:3], carry[:, 1, 0:1], pm[:, 0:1], ALU.subtract))
            dve.sem_inc(to_act, 1)
            applied()
            link(dve.tensor_scalar(edge_new[:, 0:TW], edge_row[:, 0:TW], pm[:, 1:2], None, ALU.mult))
            dve.tensor_copy(edge_new[:, SW - 1:SW], pm[:, 0:1])
            dve.scalar_tensor_tensor(out=edge_new[:, 0:TW], in0=carry[:, 0, :], scalar=pm[:, 2:3],
                                     in1=edge_new[:, 0:TW], op0=ALU.mult, op1=ALU.add)\
               .then_inc(edge_new_ready, 1)

            for b in range(NBATCH):
                js = slice(b * BJ, (b + 1) * BJ)
                dve.wait_ge(batch_in[1][b], 16 * BJ)
                link(dve.reciprocal(qq[4], agg1[0:NP_, js, D:TW].rearrange("p j o -> p (j o)")))
                link(dve.tensor_tensor(qq[5], qq[4], has[0:NP_, js], ALU.mult))
                link(dve.tensor_tensor(vv[0], agg1[0:NP_, js, 0:D], bc(qq[5]), ALU.mult))
                link(dve.tensor_tensor(vv[1], vv[0], h1[0:NP_, js, 0:D], ALU.add))
                layernorm(xs[0:NP_, js, :]).then_inc(out_ready, 1)
                dve.wait_ge(out_ready, b + 1)


def kernel(**inputs):
    import numpy as np
    import concourse.bacc as bacc
    from concourse.bass_utils import run_bass_kernel_spmd

    get = {k: np.asarray(a) for k, a in inputs.items()}
    x, src, dst = get["x"], get["src"], get["dst"]
    src_t = np.zeros((P, TPAD), src.dtype)
    src_t[:, 0:T] = src.reshape(P, T)
    radial_t = np.zeros((NB, TPAD, P), get["edge_attr_8"].dtype)
    radial_t[:, 0:T, :] = get["edge_attr_8"].reshape(P, T, NB).transpose(2, 1, 0)

    def columns(w):
        w = w.reshape(-1, 4, MUL, MUL).transpose(0, 1, 3, 2)
        first = np.stack([w[:, 1], w[:, 0]], axis=2)
        parts = [a.reshape(a.shape[0], -1) for a in (first, w[:, 2], w[:, 3])]
        return np.concatenate(parts, axis=1)

    w_self = np.zeros((D, D), get["L0_gnn_Ws"].dtype)
    w_self[0:MUL, 0:MUL] = get["L0_gnn_Ws"]
    for i in range(3):
        w_self[MUL + i::3, MUL + i::3] = get["L0_gnn_Wv"]
    base = np.zeros((P, 2), np.float32)
    base[:, 0] = [p * T for p in range(P)]
    base[:, 1] = [p * NJ - 0.5 for p in range(P)]
    edges = dst.reshape(P, T)
    arrays = dict(
        x=x, x_t=x.reshape(NP_, NJ, D).transpose(2, 1, 0), src=src_t, dst=dst,
        dst_firsts=dst.reshape(FIRSTS, ROW)[:, 0].reshape(1, FIRSTS),
        dst_edges=np.stack([edges[:, 0], edges[:, T - 1]]),
        sh=get["edge_attr_4"].reshape(P, 4 * T), radial_t=radial_t.reshape(NB, TPAD * P),
        w1=get["L0_gnn_W1"], b1=get["L0_gnn_b1"].reshape(HR, 1), w2=get["L0_gnn_W2"],
        b2=get["L0_gnn_b2"].reshape(HR, 1), w3=columns(get["L0_gnn_W3"]),
        b3=columns(get["L0_gnn_b3"].reshape(1, NTP)), w_self=w_self,
        attn=get["L1_gnn_attn_w"].reshape(1, 2 * D), base=base)
    arrays = {f"in_{k}": np.ascontiguousarray(a) for k, a in arrays.items()}
    nc = bacc.Bacc("TRN2", target_bir_lowering=False, num_devices=1)
    args = [nc.dram_tensor(k, a.shape, mybir.dt.from_np(a.dtype), kind="ExternalInput").ap()
            for k, a in arrays.items()]
    args.append(nc.dram_tensor("out_nodes", (N, D), F32, kind="ExternalOutput").ap())
    build(nc, *args)
    r = run_bass_kernel_spmd(nc, [arrays], core_ids=[0])
    return r.results[0]["out_nodes"]
```
